# Optimizing a Trainium2 kernel written in Bass

```python
import numpy as np
import jax
import jax.numpy as jnp

def _softmax(x, axis=-1):
    return jax.nn.softmax(x, axis=axis)

def _gelu(x):
    return jax.nn.gelu(x, approximate=True)

def _silu(x):
    return jax.nn.silu(x)

def _sigmoid(x):
    return jax.nn.sigmoid(x)

def _layernorm(x, axis=-1, eps=1e-05):
    m = jnp.mean(x, axis=axis, keepdims=True)
    v = jnp.var(x, axis=axis, keepdims=True)
    return (x - m) / jnp.sqrt(v + eps)

def _scatter_add(tgt, idx, src, axis=0):
    return tgt.at[idx].add(src)

def _segment_sum(src, seg, n):
    return jax.ops.segment_sum(src, seg, n)
kernel_name = 'mk_seq_preln_d1_jaxref_r8_e5c564'

def setup_inputs(seed: int=0):
    np.random.seed(seed)
    _w = jnp.asarray

    def _L0_attn_setup():
        import jax, jax.numpy as jnp
        import numpy as np
        B, T, H, S, F, G = (2, 256, 512, 128, 1248, 6)
        GRAD_ORDER_MIN = 4
        THD = 2.5
        key = jax.random.key(seed)
        ks = jax.random.split(key, 9)
        sc = 0.02
        hidden_states = jax.random.normal(ks[0], (B, T, H), jnp.float32)
        up_w = jax.random.normal(ks[1], (S, H), jnp.float32) * sc
        gate_w = jax.random.normal(ks[2], (S, H), jnp.float32) / np.sqrt(H)
        local_point = jax.random.normal(ks[3], (S,), jnp.float32)
        local_approx_output = jax.random.normal(ks[4], (H, S), jnp.float32) * sc
        fuse_weight = jax.random.normal(ks[5], (H, S, G), jnp.float32) * sc
        discount_factor = jnp.asarray(np.cumsum(np.log(np.arange(1, G + 1, dtype=np.float64))), jnp.float32)
        ffn_gate_w = jax.random.normal(ks[6], (F, H), jnp.float32) * sc
        ffn_up_w = jax.random.normal(ks[7], (F, H), jnp.float32) * sc
        ffn_down_w = jax.random.normal(ks[8], (H, F), jnp.float32) * sc
        return {'hidden_states': hidden_states, 'up_w': up_w, 'gate_w': gate_w, 'local_point': local_point, 'local_approx_output': local_approx_output, 'fuse_weight': fuse_weight, 'discount_factor': discount_factor, 'ffn_gate_w': ffn_gate_w, 'ffn_up_w': ffn_up_w, 'ffn_down_w': ffn_down_w}
    _L0_attn_in = _L0_attn_setup()

    def _L0_ffn_setup():
        import jax, jax.numpy as jnp
        import numpy as np
        GROUP_SIZE = 32
        OUT_F, IN_F = (512, 512)
        key = jax.random.key(seed)
        k1, k2, k3, k4, k5 = jax.random.split(key, 5)
        x = jax.random.normal(k1, (4, 256, IN_F), dtype=jnp.float32)
        qweight = jax.random.randint(k2, (OUT_F, IN_F), 0, 32, dtype=jnp.int32)
        n_groups = OUT_F * IN_F // GROUP_SIZE
        scales = jax.random.uniform(k3, (n_groups, 1), dtype=jnp.float32, minval=0.0001, maxval=0.001)
        zeros = jax.random.randint(k4, (n_groups, 1), 0, 32).astype(jnp.float32)
        bias = jax.random.normal(k5, (OUT_F,), dtype=jnp.float32)
        return {'x': x, 'qweight': qweight, 'scales': scales, 'zeros': zeros, 'bias': bias}
    _L0_ffn_in = _L0_ffn_setup()
    _d = {'L0_attn_hidden_states': _L0_attn_in['hidden_states'], 'L0_attn_up_w': _L0_attn_in['up_w'], 'L0_attn_gate_w': _L0_attn_in['gate_w'], 'L0_attn_local_point': _L0_attn_in['local_point'], 'L0_attn_local_approx_output': _L0_attn_in['local_approx_output'], 'L0_attn_fuse_weight': _L0_attn_in['fuse_weight'], 'L0_attn_discount_factor': _L0_attn_in['discount_factor'], 'L0_attn_ffn_gate_w': _L0_attn_in['ffn_gate_w'], 'L0_attn_ffn_up_w': _L0_attn_in['ffn_up_w'], 'L0_attn_ffn_down_w': _L0_attn_in['ffn_down_w'], 'L0_ffn_qweight': _L0_ffn_in['qweight'], 'L0_ffn_scales': _L0_ffn_in['scales'], 'L0_ffn_zeros': _L0_ffn_in['zeros'], 'L0_ffn_bias': _L0_ffn_in['bias']}
    _x0 = _d['L0_attn_hidden_states']
    _d['L0_attn_hidden_states'] = jax.random.normal(jax.random.fold_in(jax.random.key(seed), 1), (4, 512, 512), dtype=_x0.dtype)
    del _x0
    return _d

def reference(L0_attn_hidden_states, L0_attn_up_w, L0_attn_gate_w, L0_attn_local_point, L0_attn_local_approx_output, L0_attn_fuse_weight, L0_attn_discount_factor, L0_attn_ffn_gate_w, L0_attn_ffn_up_w, L0_attn_ffn_down_w, L0_ffn_qweight, L0_ffn_scales, L0_ffn_zeros, L0_ffn_bias):

    def _L0_attn_ref(hidden_states, up_w, gate_w, local_point, local_approx_output, fuse_weight, discount_factor, ffn_gate_w, ffn_up_w, ffn_down_w):
        import jax, jax.numpy as jnp
        import numpy as np
        B, T, H, S, F, G = (2, 256, 512, 128, 1248, 6)
        GRAD_ORDER_MIN = 4
        THD = 2.5
        approx_up = hidden_states @ up_w.T
        gate_pre = hidden_states @ gate_w.T
        delta = gate_pre - local_point
        neg_factor = jnp.where(delta > 0, 1.0, -1.0).astype(hidden_states.dtype)
        delta_abs = jnp.abs(delta)
        log_delta = jnp.log(delta_abs)
        keep = (delta_abs <= THD).astype(hidden_states.dtype)
        approx_out = approx_up @ local_approx_output.T
        for idx in range(G):
            m = idx + 1
            dterm = jnp.exp(log_delta * m - discount_factor[idx])
            if m % 2 == 1:
                dterm = dterm * neg_factor
            tmp = dterm * approx_up
            if m > GRAD_ORDER_MIN:
                tmp = tmp * keep
            approx_out = approx_out + tmp @ fuse_weight[:, :, idx].T
        ffn_out = jax.nn.silu(hidden_states @ ffn_gate_w.T) * (hidden_states @ ffn_up_w.T) @ ffn_down_w.T
        return approx_out + ffn_out

    def _L0_ffn_ref(x, qweight, scales, zeros, bias):
        import jax, jax.numpy as jnp
        import numpy as np
        GROUP_SIZE = 32
        OUT_F, IN_F = (512, 512)
        w = qweight.astype(x.dtype).reshape(-1, GROUP_SIZE)
        w = (w - zeros) * scales
        w = w.reshape(OUT_F, IN_F)
        return jnp.einsum('bsi,oi->bso', x, w) + bias
    x = L0_attn_hidden_states
    x = x + _L0_attn_ref(_layernorm(x, axis=-1), L0_attn_up_w, L0_attn_gate_w, L0_attn_local_point, L0_attn_local_approx_output, L0_attn_fuse_weight, L0_attn_discount_factor, L0_attn_ffn_gate_w, L0_attn_ffn_up_w, L0_attn_ffn_down_w)
    x = x + _L0_ffn_ref(_layernorm(x, axis=-1), L0_ffn_qweight, L0_ffn_scales, L0_ffn_zeros, L0_ffn_bias)
    return x

_drawn_inputs = setup_inputs


def setup_inputs(seed=0):
    import zlib

    import numpy as np

    out = dict(_drawn_inputs(seed))
    spreads = {}
    factors = {}
    for name, (base, spread) in spreads.items():
        noise = np.random.default_rng([zlib.crc32(name.encode()), seed]).standard_normal(out[name].shape)
        drawn = base * np.exp(spread * noise) if base else spread * noise
        out[name] = jnp.asarray(drawn.astype(out[name].dtype))
    for name, factor in factors.items():
        out[name] = (out[name] * factor).astype(out[name].dtype)
    return out
```

```python
from contextlib import ExitStack

import concourse.bass as bass
from concourse import mybir

P = 128
ALU = mybir.AluOpType
ACT = mybir.ActivationFunctionType
F32 = mybir.dt.float32
F32R = mybir.dt.float32r
I32 = mybir.dt.int32

THD = 2.5
GRAD_ORDER_MIN = 4
EPS = 1e-5
QGROUP = 32


def block_kernel(nc, x, gate_up_w, down_w, local_point, discount, q_w, q_scales, q_zeros, bias, out):
    T, H = x.shape
    TILES = T // P
    GT = 4
    GROUPS = TILES // GT
    GN = GT * P
    K = H // P
    GU_CHUNKS = gate_up_w.shape[0]
    FFN_CHUNKS = GU_CHUNKS - 1
    PAIRS = FFN_CHUNKS // 2
    POWERS = down_w.shape[0] - FFN_CHUNKS
    GUW = K * P
    BRANCH = FFN_CHUNKS
    assert H == GN == 512 and GROUPS == 4 and FFN_CHUNKS % 2 == 0 and POWERS == 7

    USE_DOWN = GROUPS * K
    USE_LAST = USE_DOWN + PAIRS * TILES
    USES = 3 * GT

    def step(chunk, g):
        return GROUPS * chunk + g

    with ExitStack() as ctx:
        def sb(name, shape, dt):
            return ctx.enter_context(nc.sbuf_tensor(name, shape, dt))

        def bank(name):
            return ctx.enter_context(nc.psum_tensor(name, [P, 512], F32))

        def sem(name):
            return ctx.enter_context(nc.semaphore(name))

        X = sb("X", [P, TILES, H], F32)
        xT_hi = sb("xT_hi", [P, K, GROUPS, GN], F32R)
        xT_lo = sb("xT_lo", [P, K, GROUPS, GN], F32R)
        x2T_hi, x2T_lo = xT_hi[:, :, 0, :], xT_lo[:, :, 0, :]
        hT = sb("hT", [P, GROUPS, 2, 2, GN], F32R)
        rT = hT[:, :, :, :, :].rearrange("p g c s n -> p (g c s) n")
        gu_w = sb("gu_w", [P, 2, 2, 2, GUW], F32R)
        d_w = sb("d_w", [P, 2, 2, H], F32R)
        fuse_w = sb("fuse_w", [P, POWERS, 2, H], F32R)
        gu_raw = sb("gu_raw", [P, 2, 2 * GUW], F32)
        d_raw = sb("d_raw", [P, 2, H], F32)
        sg = sb("sg", [P, 2, GN], F32)
        hf = sb("hf", [P, 2, GN], F32)
        xhat = sb("xhat", [P, 2, H], F32)
        bias_sb = sb("bias_sb", [P, H], F32)
        ident = sb("ident", [P, P], F32)
        bn = sb("bn", [P, 2, 6], F32)
        mean_var = sb("mean_var", [P, GT, 2], F32)
        var_eps = sb("var_eps", [P, GT], F32)
        rstd = sb("rstd", [P, GT], F32)
        minus_half = sb("minus_half", [P, 1], F32)
        eps = sb("eps", [P, 1], F32)
        lp = sb("lp", [P, 1], F32)
        disc = sb("disc", [P, POWERS - 1], F32)
        coef = sb("coef", [P, POWERS - 1], F32)
        delta, abs_delta = sg[:, 0, :], sg[:, 1, :]
        power = [hf[:, 0, :], hf[:, 1, :], d_raw[:, 0, :], d_raw[:, 1, :]]
        q_stage = gu_raw[:, :, :].rearrange("p s (a n) -> p (s a) n", n=H)
        q_int = q_stage[:, 0, :].bitcast(I32)
        q_zero, q_scale, q_val = q_stage[:, 1, :], q_stage[:, 2, :], q_stage[:, 3, :]

        def q_split(k, part):
            return gu_w[:, 1, part, k, :] if k < 2 else d_w[:, k - 2, part, :]

        row_bank = [bank(f"row_bank{i}") for i in range(4)]
        bank_a = [bank(f"bank_a{i}") for i in range(2)]
        bank_b = [bank(f"bank_b{i}") for i in range(2)]

        x_loaded = [sem(f"x_loaded{i}") for i in range(GT + GROUPS - 1)]
        params_loaded = sem("params_loaded")
        gu_loaded = [sem(f"gu_loaded{i}") for i in range(2)]
        d_loaded = [sem(f"d_loaded{i}") for i in range(2)]
        q_loaded = sem("q_loaded")
        ident_step = sem("ident_step")
        ident_ready = sem("ident_ready")
        bn_ready = sem("bn_ready")
        mean_ready = sem("mean_ready")
        var_eps_ready = sem("var_eps_ready")
        rstd_ready = sem("rstd_ready")
        xhat_ready = sem("xhat_ready")
        xhat_turned = sem("xhat_turned")
        row_ready = sem("row_ready")
        row_drained = sem("row_drained")
        xT_hi_ready = sem("xT_hi_ready")
        coef_ready = sem("coef_ready")
        gu_hi = sem("gu_hi")
        gu_lo = sem("gu_lo")
        d_scaled = sem("d_scaled")
        d_hi = sem("d_hi")
        d_lo = sem("d_lo")
        gu_done = sem("gu_done")
        a_read = sem("a_read")
        b_read = sem("b_read")
        h_hi = sem("h_hi")
        h_lo = sem("h_lo")
        abs_ready = sem("abs_ready")
        power_ready = sem("power_ready")
        r_hi = sem("r_hi")
        r_lo_pool = sem("r_lo_pool")
        r_lo_dve = sem("r_lo_dve")
        q_cast = sem("q_cast")
        q_sub = sem("q_sub")
        q_mul = sem("q_mul")
        q_hi = sem("q_hi")
        q_lo = sem("q_lo")
        bias_added = sem("bias_added")
        stored = sem("stored")
        POOL_POWERS = 4
        DVE_POWERS = POWERS - POOL_POWERS
        CHAIN = POWERS

        block = ctx.enter_context(nc.Block())

        def rows(g, i):
            return (g * GT + i) * P

        @block.sync
        def _(sp):
            def load_gu(q, slot):
                sp.dma_start(gu_raw[:, slot, :], gate_up_w[q, :, :]).then_inc(gu_loaded[slot], 16)

            def load_d(q, slot):
                sp.dma_start(d_raw[:, slot, :], down_w[q, :, :]).then_inc(d_loaded[slot], 16)

            for i in range(GT):
                sp.dma_start(X[:, i, :], x[i * P:(i + 1) * P, :]).then_inc(x_loaded[i], 16)
            load_gu(0, 0)

            def load_x(g):
                sp.dma_start(X[:, g * GT:(g + 1) * GT, :],
                             x[g * GN:(g + 1) * GN, :].rearrange("(t p) n -> p t n", p=P)) \
                    .then_inc(x_loaded[GT + g - 1], 16)

            load_x(1)
            load_gu(1, 1)
            load_x(2)
            load_x(3)
            load_d(0, 0)
            load_d(1, 1)
            sp.dma_start(bias_sb[:, :], bias.unsqueeze(0).to_broadcast([P, H])).then_inc(params_loaded, 16)
            with sp.Fori(0, PAIRS - 1) as p:
                for c in range(2):
                    sp.wait_ge(gu_lo, 2 * p + c + 1)
                    load_gu(2 * p + 2 + c, c)
                for c in range(2):
                    sp.wait_ge(d_lo, 2 * p + c + 1)
                    load_d(2 * p + 2 + c, c)
            sp.wait_ge(gu_lo, FFN_CHUNKS - 1)
            load_gu(BRANCH, 0)
            for q in range(FFN_CHUNKS, FFN_CHUNKS + POWERS):
                sp.wait_ge(d_lo, q - 1)
                load_d(q, q % 2)
            sp.wait_ge(gu_lo, GU_CHUNKS)
            per = P // QGROUP
            for k in range(K):
                if k >= 1:
                    sp.wait_ge(q_mul, k)
                sp.dma_start(q_int, q_w[k * P:(k + 1) * P, :]).then_inc(q_loaded, 16)
                for dst, src in ((q_zero, q_zeros), (q_scale, q_scales)):
                    sp.dma_start(dst, src[k * per:(k + 1) * per, :].unsqueeze(1)
                                 .to_broadcast([per, QGROUP, H])).then_inc(q_loaded, 16)
            with sp.Fori(0, GROUPS) as g:
                for i in range(GT):
                    sp.wait_ge(row_drained, USE_LAST + USES * g + 2 * GT + i + 1)
                    sp.dma_start(out[bass.ds(rows(g, i), P), :], X[:, g * GT + i, :]).then_inc(stored, 16)
            sp.wait_ge(stored, 16 * TILES)

        @block.gpsimd
        def _(pool):
            pool.memset(ident[:, :], 0.0).then_inc(ident_step, 1)
            pool.memset(minus_half[:, :], -0.5).then_inc(ident_step, 1)
            pool.memset(eps[:, :], EPS).then_inc(ident_step, 1)
            pool.wait_ge(ident_step, 3)
            pool.affine_select(out=ident[:, :], in_=ident[:, :], compare_op=ALU.not_equal, fill=1.0,
                               base=0, pattern=[[-1, P]], channel_multiplier=1).then_inc(ident_ready, 1)

            def inv_std(n, i):
                pool.wait_ge(mean_ready, n + 1)
                if not (isinstance(n, int) and n < GT):
                    pool.wait_ge(xhat_ready, n - GT + 1)
                pool.tensor_tensor(var_eps[:, i:i + 1], mean_var[:, i, 1:2], eps[:, :], ALU.add) \
                    .then_inc(var_eps_ready, 1)
                pool.wait_ge(var_eps_ready, n + 1)
                pool.tensor_tensor(rstd[:, i:i + 1], var_eps[:, i:i + 1], minus_half[:, :], ALU.pow) \
                    .then_inc(rstd_ready, 1)

            def split_lo(dst, src, hi):
                return pool.tensor_tensor(dst, src, hi.bitcast(F32), ALU.subtract)

            def split_gu(q, slot):
                pool.wait_ge(gu_hi, q + 1)
                split_lo(gu_w[:, slot, 1, :, :].rearrange("p a n -> p (a n)"), gu_raw[:, slot, :],
                         gu_w[:, slot, 0, :, :].rearrange("p a n -> p (a n)")).then_inc(gu_lo, 1)

            def split_d(q, slot):
                pool.wait_ge(d_hi, q + 1)
                split_lo(d_w[:, slot, 1, :], d_raw[:, slot, :], d_w[:, slot, 0, :]).then_inc(d_lo, 1)

            for g in range(GROUPS):
                for i in range(GT):
                    inv_std(g * GT + i, i)
                if g == 0:
                    split_gu(0, 0)
                if g == 2:
                    split_gu(1, 1)
            split_d(0, 0)
            split_d(1, 1)
            with pool.Fori(0, PAIRS - 1) as p:
                split_gu(2 * p + 2, 0)
                split_gu(2 * p + 3, 1)
                for c in range(2):
                    split_d(2 * p + 2 + c, c)
            split_gu(BRANCH, 0)
            for m in range(POWERS):
                q = FFN_CHUNKS + m
                if m >= 1:
                    pool.wait_ge(d_loaded[q % 2], 16 * (q // 2 + 1))
                    if m == 1:
                        pool.wait_ge(coef_ready, 1)
                    pool.tensor_scalar(d_raw[:, q % 2, :], d_raw[:, q % 2, :], coef[:, m - 1:m], None,
                                       ALU.mult).then_inc(d_scaled, 1)
                pool.wait_ge(d_hi, q + 1)
                split_lo(fuse_w[:, m, 1, :], d_raw[:, q % 2, :], fuse_w[:, m, 0, :]).then_inc(d_lo, 1)

            def split_powers(g):
                for m in range(POOL_POWERS):
                    pool.wait_ge(r_hi, POWERS * g + m + 1)
                    split_lo(rT[:, 2 * m + 1, :], power[m], rT[:, 2 * m, :]).then_inc(r_lo_pool, 1)

            def dequantise(k):
                pool.wait_ge(q_cast, k + 1)
                pool.tensor_tensor(q_val, q_val, q_zero, ALU.subtract).then_inc(q_sub, 1)
                pool.wait_ge(q_sub, k + 1)
                pool.tensor_tensor(q_val, q_val, q_scale, ALU.mult).then_inc(q_mul, 1)
                pool.wait_ge(q_hi, k + 1)
                split_lo(q_split(k, 1), q_val, q_split(k, 0)).then_inc(q_lo, 1)

            def add_bias(g, i):
                pool.wait_ge(xhat_ready, TILES + GT * g + i + 1)
                pool.tensor_tensor(X[:, g * GT + i, :], X[:, g * GT + i, :], bias_sb[:, :], ALU.add) \
                    .then_inc(bias_added, 1)

            split_powers(0)
            pool.wait_ge(params_loaded, 48)
            for i in range(GT):
                dequantise(i)
                inv_std(TILES + i, i)
            for i in range(GT):
                add_bias(0, i)
            split_powers(1)
            with pool.Fori(1, GROUPS - 1) as g:
                for i in range(GT):
                    inv_std(TILES + GT * g + i, i)
                for i in range(GT):
                    add_bias(g, i)
                split_powers(g + 1)
            for i in range(GT):
                inv_std(TILES + GT * (GROUPS - 1) + i, i)
            for i in range(GT):
                add_bias(GROUPS - 1, i)

        @block.scalar
        def _(act):
            act.dma_start(disc[:, :], discount.unsqueeze(0).to_broadcast([P, POWERS - 1])) \
                .then_inc(params_loaded, 16)
            act.dma_start(lp[:, :], local_point.unsqueeze(1)).then_inc(params_loaded, 16)
            def coefficients():
                act.wait_ge(params_loaded, 48)
                act.activation(coef[:, :], disc[:, :], ACT.Exp, scale=-1.0).then_inc(coef_ready, 1)

            def split_gu(q, slot, loads, steps_done):
                act.wait_ge(gu_loaded[slot], 16 * loads)
                if steps_done is not None:
                    act.wait_ge(gu_done, steps_done)
                act.activation(gu_w[:, slot, 0, :, :].rearrange("p a n -> p (a n)"), gu_raw[:, slot, :],
                               ACT.Copy).then_inc(gu_hi, 1)

            def split_d(slot, loads, uses_done):
                act.wait_ge(d_loaded[slot], 16 * loads)
                if uses_done is not None:
                    act.wait_ge(row_ready, uses_done)
                act.activation(d_w[:, slot, 0, :], d_raw[:, slot, :], ACT.Copy).then_inc(d_hi, 1)

            def split_fuse(m):
                q = FFN_CHUNKS + m
                if m == 0:
                    act.wait_ge(d_loaded[q % 2], 16 * (q // 2 + 1))
                else:
                    act.wait_ge(d_scaled, m)
                act.activation(fuse_w[:, m, 0, :], d_raw[:, q % 2, :], ACT.Copy).then_inc(d_hi, 1)

            def xT_hi_group(use, nth, dst):
                for k in range(K):
                    act.wait_ge(row_ready, use + k + 1)
                    act.activation(dst[k], row_bank[k][:, :], ACT.Copy).then_inc(xT_hi_ready, 1)

            def ffn_step(n, g, c, uses_done):
                act.wait_ge(gu_done, n + 1)
                if not (isinstance(n, int) and n < 2):
                    act.wait_ge(b_read, n - 1)
                act.activation(sg[:, g % 2, :], bank_a[g % 2][:, :], ACT.Silu).then_inc(a_read, 1)
                act.wait_ge(b_read, n + 1)
                if uses_done is not None:
                    act.wait_ge(row_ready, uses_done)
                act.activation(hT[:, g, c, 0, :], hf[:, g % 2, :], ACT.Copy).then_inc(h_hi, 1)

            split_gu(0, 0, 1, None)
            xT_hi_group(0, 0, [xT_hi[:, k, 0, :] for k in range(K)])
            for g in range(GROUPS):
                if g + 1 < GROUPS:
                    xT_hi_group((g + 1) * K, g + 1, [xT_hi[:, k, g + 1, :] for k in range(K)])
                if g == 1:
                    split_gu(1, 1, 1, None)
                if g == 2:
                    split_d(0, 1, None)
                    split_d(1, 1, None)
                ffn_step(step(0, g), g, 0, None)

            def pair_steps(p, between):
                for g in range(GROUPS):
                    ffn_step(step(2 * p + 1, g), g, 1, USE_DOWN + TILES * (p - 1) + GT * (g + 1))
                    between(g)

            with act.Fori(0, PAIRS - 1) as p:
                def between(g):
                    if g == 0:
                        split_gu(2 * p + 2, 0, p + 2, step(2 * p + 1, 0))
                pair_steps(p, between)
                split_gu(2 * p + 3, 1, p + 2, step(2 * p + 2, 0))
                for g in range(GROUPS):
                    ffn_step(step(2 * p + 2, g), g, 0, USE_DOWN + TILES * p + GT * (g + 1))
                    if g == 0:
                        for c in range(2):
                            split_d(c, p + 2, USE_DOWN + TILES * (p + 1))

            def between_last(g):
                if g == 0:
                    split_gu(BRANCH, 0, PAIRS + 1, step(BRANCH - 1, 0))
                    coefficients()
                    split_fuse(0)
                elif g == GROUPS - 1:
                    split_fuse(5)
                    split_fuse(6)
                else:
                    split_fuse(2 * g - 1)
                    split_fuse(2 * g)

            pair_steps(PAIRS - 1, between_last)

            def branch_copy(g):
                n = step(BRANCH, 0) + g
                act.wait_ge(gu_done, n + 1)
                if isinstance(g, int) and g == 0:
                    act.wait_ge(h_lo, step(BRANCH, 0))
                else:
                    act.wait_ge(power_ready, CHAIN * g)
                    act.wait_ge(r_lo_dve, DVE_POWERS * g)
                    act.wait_ge(r_lo_pool, POOL_POWERS * g)
                return n

            def powers_hi(g, first):
                for m in range(POWERS):
                    if m == 0:
                        act.wait_ge(a_read, step(BRANCH, 0) + g + 1)
                    elif m == 1:
                        act.wait_ge(b_read, step(BRANCH, 0) + g + 1)
                        act.activation(abs_delta, delta, ACT.Abs).then_inc(abs_ready, 1)
                        act.wait_ge(power_ready, CHAIN * g + 1)
                    else:
                        act.wait_ge(power_ready, CHAIN * g + (m if m <= GRAD_ORDER_MIN else m + 1))
                    if first:
                        act.wait_ge(row_ready, USE_LAST - TILES + GT * (m // 2 + 1))
                    elif m == 0:
                        act.wait_ge(row_ready, USE_LAST + USES * (g - 1) + GT)
                    act.activation(rT[:, 2 * m, :], power[m % 4 if m <= GRAD_ORDER_MIN else m - 3],
                                   ACT.Copy).then_inc(r_hi, 1)

            def copy_up(g, slot):
                branch_copy(g)
                act.activation(power[0], bank_a[slot][:, :], ACT.Copy).then_inc(a_read, 1)

            def linear_hi(k):
                act.wait_ge(q_loaded, 48 * (k + 1))
                if k >= 1:
                    act.wait_ge(q_lo, k)
                act.activation(q_val, q_int, ACT.Copy).then_inc(q_cast, 1)
                act.wait_ge(q_mul, k + 1)
                if k == 0:
                    act.wait_ge(gu_done, step(BRANCH, 0))
                if k == 2:
                    act.wait_ge(row_ready, USE_LAST)
                act.activation(q_split(k, 0), q_val, ACT.Copy).then_inc(q_hi, 1)

            def x2T_hi_group(g):
                xT_hi_group(USE_LAST + USES * g + GT, 0, [x2T_hi[:, k, :] for k in range(K)])

            copy_up(0, 0)
            powers_hi(0, True)
            for k in range(K):
                linear_hi(k)
            act.wait_ge(gu_done, step(BRANCH, 0) + 1)
            copy_up(1, 1)
            x2T_hi_group(0)
            powers_hi(1, False)
            for g in range(1, GROUPS - 1):
                copy_up(g + 1, (g + 1) % 2)
                act.wait_ge(row_ready, USE_LAST + USES * g)
                x2T_hi_group(g)
                powers_hi(g + 1, False)
            act.wait_ge(row_ready, USE_LAST + USES * (GROUPS - 1))
            x2T_hi_group(GROUPS - 1)

        @block.tensor
        def _(pe):
            def product(ps, pairs, k_first, k_last, done):
                for j, (a, b) in enumerate(pairs):
                    mm = pe.matmul(ps, a, b, start=(k_first and j == 0),
                                   stop=(k_last and j == len(pairs) - 1))
                if done is not None:
                    mm.then_inc(done, 1)

            def gate_up(n, slot, g, parity, first_wait, xT_wait, hook):
                if first_wait is not None:
                    pe.wait_ge(gu_lo, first_wait)
                if not (isinstance(n, int) and n < 2):
                    pe.wait_ge(a_read, n - 1)
                    pe.wait_ge(b_read, n - 1)
                for b, ps in enumerate((bank_a[parity], bank_b[parity])):
                    for k in range(K):
                        if xT_wait and b == 0:
                            pe.wait_ge(row_drained, g * K + k + 1)
                        w_hi = gu_w[:, slot, 0, b, k * P:(k + 1) * P]
                        w_lo = gu_w[:, slot, 1, b, k * P:(k + 1) * P]
                        x_hi, x_lo = xT_hi[:, k, g, :], xT_lo[:, k, g, :]
                        last = b == 1 and k == K - 1
                        product(ps[:, :], [(w_hi, x_hi), (w_hi, x_lo), (w_lo, x_hi)],
                                k == 0, k == K - 1, gu_done if last else None)
                        hook(b * K + k)

            def turn(use, tile, i):
                pe.wait_ge(xhat_ready, tile + 1)
                if i == 0 and not (isinstance(use, int) and use == 0):
                    pe.wait_ge(row_drained, use)
                for k in range(K):
                    mm = pe.transpose(row_bank[k][:, i * P:(i + 1) * P], xhat[:, i % 2, k * P:(k + 1) * P],
                                      ident[:, :])
                    if i == GT - 1:
                        mm.then_inc(row_ready, 1)
                if i < GT - 1:
                    mm.then_inc(xhat_turned, 1)

            def no_hook(j):
                pass

            def down(p, g):
                for i in range(GT):
                    use = USE_DOWN + TILES * p + GT * g + i
                    if i == 0:
                        pe.wait_ge(h_lo, step(2 * p + 1, g) + 1)
                        if g == 0:
                            pe.wait_ge(d_lo, 2 * p + 2)
                    pe.wait_ge(row_drained, use - 3)
                    for c in range(2):
                        a_hi = hT[:, g, c, 0, i * P:(i + 1) * P]
                        a_lo = hT[:, g, c, 1, i * P:(i + 1) * P]
                        product(row_bank[i][:, :], [(a_hi, d_w[:, c, 0, :]), (a_hi, d_w[:, c, 1, :]),
                                                    (a_lo, d_w[:, c, 0, :])], c == 0, c == 1,
                                row_ready if c == 1 else None)

            def fuse(g):
                pe.wait_ge(r_lo_pool, POOL_POWERS * (g + 1))
                pe.wait_ge(r_lo_dve, DVE_POWERS * (g + 1))
                if isinstance(g, int) and g == 0:
                    pe.wait_ge(d_lo, FFN_CHUNKS + POWERS)
                for i in range(GT):
                    pe.wait_ge(row_drained, USE_LAST + USES * g + i - 3)
                    for m in range(POWERS):
                        a_hi = rT[:, 2 * m, i * P:(i + 1) * P]
                        a_lo = rT[:, 2 * m + 1, i * P:(i + 1) * P]
                        last = m == POWERS - 1
                        product(row_bank[i][:, :], [(a_hi, fuse_w[:, m, 0, :]), (a_hi, fuse_w[:, m, 1, :]),
                                                    (a_lo, fuse_w[:, m, 0, :])], m == 0, last,
                                row_ready if last else None)

            def linear(g):
                pe.wait_ge(row_drained, USE_LAST + USES * g + 2 * GT)
                if isinstance(g, int) and g == 0:
                    pe.wait_ge(q_lo, K)
                for i in range(GT):
                    for k in range(K):
                        a_hi = x2T_hi[:, k, i * P:(i + 1) * P]
                        a_lo = x2T_lo[:, k, i * P:(i + 1) * P]
                        w_hi, w_lo = q_split(k, 0), q_split(k, 1)
                        product(row_bank[i][:, :], [(a_hi, w_hi), (a_hi, w_lo), (a_lo, w_hi)],
                                k == 0, k == K - 1, row_ready if k == K - 1 else None)

            pe.wait_ge(ident_ready, 1)
            for i in range(GT):
                turn(0, i, i)
            for g in range(GROUPS):
                def hook(j):
                    if g + 1 < GROUPS and j % 2 == 1:
                        if j == 1:
                            pass
                        turn((g + 1) * K, (g + 1) * GT + j // 2, j // 2)
                gate_up(step(0, g), 0, g, g % 2, 1 if g == 0 else None, True, hook)

            def pair(p, branch):
                for g in range(GROUPS):
                    gate_up(step(2 * p + 1, g), 1, g, g % 2, 2 * p + 2 if g == 0 else None, False, no_hook)
                    if g in (1, 2):
                        down(p, g - 1)
                if branch:
                    gate_up(step(BRANCH, 0), 0, 0, 0, GU_CHUNKS, False, no_hook)
                down(p, 2)
                down(p, 3)

            with pe.Fori(0, PAIRS - 1) as p:
                pair(p, False)
                for g in range(GROUPS):
                    gate_up(step(2 * p + 2, g), 0, g, g % 2, 2 * p + 3 if g == 0 else None, False, no_hook)
            pair(PAIRS - 1, True)
            for g in range(GROUPS):
                fuse(g)
                use = USE_LAST + USES * g + GT
                tile = TILES + GT * g

                def hook(j):
                    if j % 2 == 1:
                        turn(use, tile + j // 2, j // 2)
                if g + 1 < GROUPS:
                    gate_up(step(BRANCH, 0) + g + 1, 0, g + 1, (g + 1) % 2, None, False, hook)
                else:
                    for i in range(GT):
                        turn(use, tile + i, i)
                linear(g)

        @block.vector
        def _(dve):
            def stats(n, tile, i):
                if not (isinstance(n, int) and n < 2):
                    dve.wait_ge(mean_ready, n - 1)
                dve.bn_stats(bn[:, i % 2, :], X[:, tile, :]).then_inc(bn_ready, 1)
                dve.wait_ge(bn_ready, n + 1)
                if not (isinstance(n, int) and n < GT):
                    dve.wait_ge(xhat_ready, n - GT + 1)
                    dve.wait_ge(var_eps_ready, n - GT + 1)
                dve.bn_aggr(mean_var[:, i, :], bn[:, i % 2, :]).then_inc(mean_ready, 1)

            def normalise(n, tile, i, turned, use_before):
                dve.wait_ge(rstd_ready, n + 1)
                if turned is not None:
                    dve.wait_ge(xhat_turned, turned)
                if use_before is not None:
                    dve.wait_ge(row_ready, use_before)
                dve.tensor_scalar(xhat[:, i % 2, :], X[:, tile, :], mean_var[:, i, 0:1], rstd[:, i:i + 1],
                                  ALU.subtract, ALU.mult).then_inc(xhat_ready, 1)

            def xT_lo_group(use, hi, dst, src):
                for k in range(K):
                    dve.wait_ge(xT_hi_ready, hi + k + 1)
                    dve.tensor_tensor(dst[k], row_bank[k][:, :], src[k].bitcast(F32), ALU.subtract) \
                        .then_inc(row_drained, 1)

            def ffn_h(n, g, c):
                dve.wait_ge(a_read, n + 1)
                if not (isinstance(n, int) and n < 2):
                    dve.wait_ge(h_hi, n - 1)
                    dve.wait_ge(h_lo, n - 1)
                dve.tensor_tensor(hf[:, g % 2, :], bank_b[g % 2][:, :], sg[:, g % 2, :], ALU.mult) \
                    .then_inc(b_read, 1)
                dve.wait_ge(h_hi, n + 1)
                dve.wait_ge(b_read, n + 1)
                dve.tensor_tensor(hT[:, g, c, 1, :], hf[:, g % 2, :], hT[:, g, c, 0, :].bitcast(F32),
                                  ALU.subtract).then_inc(h_lo, 1)

            def accumulate(use, tile, i):
                dve.wait_ge(row_ready, use + 1)
                dve.wait_ge(row_drained, use)
                dve.tensor_tensor(X[:, tile, :], row_bank[i][:, :], X[:, tile, :], ALU.add) \
                    .then_inc(row_drained, 1)

            def norm1(g):
                for i in range(GT + 1):
                    if i < GT:
                        n = g * GT + i
                        if g == 0 or i == 0:
                            dve.wait_ge(x_loaded[i if g == 0 else GT + g - 1], 16)
                        stats(n, n, i)
                    if i >= 1:
                        n = g * GT + i - 1
                        turned = use_before = None
                        if i - 1 >= 2:
                            turned = 3 * g + i - 2
                        elif g >= 1:
                            turned = 3 * g
                            use_before = K * g if i - 1 == 1 else None
                        normalise(n, n, i - 1, turned, use_before)

            def norm1_turned(g):
                xT_lo_group(K * g, K * g, [xT_lo[:, k, g, :] for k in range(K)],
                            [xT_hi[:, k, g, :] for k in range(K)])

            norm1(0)
            norm1_turned(0)
            for g in range(1, GROUPS):
                norm1(g)
                norm1_turned(g)
                ffn_h(step(0, g - 1), g - 1, 0)
            ffn_h(step(0, GROUPS - 1), GROUPS - 1, 0)

            def down_sums(p, g):
                for i in range(GT):
                    accumulate(USE_DOWN + TILES * p + GT * g + i, GT * g + i, i)

            def pair(p, last):
                for g in range(GROUPS):
                    ffn_h(step(2 * p + 1, g), g, 1)
                    if g in (1, 2):
                        down_sums(p, g - 1)
                if last:
                    chain(0, 0)
                down_sums(p, 2)
                if last:
                    powers_lo(0, [4, 5])
                down_sums(p, 3)
                if last:
                    powers_lo(0, [6])

            def chain(g, slot):
                n = step(BRANCH, 0) + g
                dve.wait_ge(gu_done, n + 1)
                first = isinstance(g, int) and g == 0
                if first:
                    dve.wait_ge(params_loaded, 48)
                    dve.wait_ge(b_read, n)
                else:
                    dve.wait_ge(power_ready, CHAIN * g)
                dve.tensor_scalar(delta, bank_b[slot][:, :], lp[:, 0:1], None, ALU.subtract) \
                    .then_inc(b_read, 1)
                dve.wait_ge(b_read, n + 1)
                for j in range(CHAIN):
                    if j == 0:
                        dve.wait_ge(a_read, n + 1)
                    else:
                        dve.wait_ge(power_ready, CHAIN * g + j)
                    src = power[j % 4]
                    dst = power[(j + 1) % 4]
                    if j < 3:
                        if first and j == 0:
                            dve.wait_ge(h_lo, n)
                            dve.wait_ge(h_hi, n)
                        if first and j == 1:
                            dve.wait_ge(d_lo, FFN_CHUNKS + POWERS)
                        if not first and j == 0:
                            dve.wait_ge(r_hi, POWERS * g)
                            dve.wait_ge(r_lo_pool, POOL_POWERS * g)
                            dve.wait_ge(r_lo_dve, DVE_POWERS * g)
                    else:
                        dve.wait_ge(r_hi, POWERS * g + j - 2)
                        dve.wait_ge(r_lo_pool, POOL_POWERS * g + j - 2)
                    if j == GRAD_ORDER_MIN:
                        dve.wait_ge(abs_ready, g + 1)
                        dve.scalar_tensor_tensor(out=dst, in0=abs_delta, scalar=THD, in1=src,
                                                 op0=ALU.is_le, op1=ALU.mult).then_inc(power_ready, 1)
                        continue
                    dve.tensor_tensor(dst, src, delta, ALU.mult).then_inc(power_ready, 1)

            def powers_lo(g, which):
                for m in which:
                    dve.wait_ge(r_hi, POWERS * g + m + 1)
                    dve.tensor_tensor(rT[:, 2 * m + 1, :], power[m % 4 if m <= GRAD_ORDER_MIN else m - 3],
                                      rT[:, 2 * m, :].bitcast(F32), ALU.subtract).then_inc(r_lo_dve, 1)

            with dve.Fori(0, PAIRS - 1) as p:
                pair(p, False)
                for g in range(GROUPS):
                    ffn_h(step(2 * p + 2, g), g, 0)
            pair(PAIRS - 1, True)

            def last_stage(g):
                use = USE_LAST + USES * g
                for i in range(GT + 1):
                    if i < GT:
                        accumulate(use + i, GT * g + i, i)
                        dve.wait_ge(row_drained, use + i + 1)
                        stats(TILES + GT * g + i, GT * g + i, i)
                    if i >= 1:
                        turned = 3 * (GROUPS + g) + (i - 2 if i - 1 >= 2 else 0)
                        before = None
                        if i - 1 == 1:
                            before = use - GT if not (isinstance(g, int) and g == 0) else K * GROUPS
                        normalise(TILES + GT * g + i - 1, GT * g + i - 1, i - 1, turned, before)
                xT_lo_group(use + GT, K * (GROUPS + g), [x2T_lo[:, k, :] for k in range(K)],
                            [x2T_hi[:, k, :] for k in range(K)])

            def linear_sums(g):
                use = USE_LAST + USES * g + 2 * GT
                for i in range(GT):
                    dve.wait_ge(row_ready, use + i + 1)
                    dve.wait_ge(bias_added, GT * g + i + 1)
                    dve.tensor_tensor(X[:, GT * g + i, :], row_bank[i][:, :], X[:, GT * g + i, :], ALU.add) \
                        .then_inc(row_drained, 1)

            for g in range(GROUPS):
                last_stage(g)
                if g + 1 < GROUPS:
                    chain(g + 1, (g + 1) % 2)
                    powers_lo(g + 1, [4, 5, 6])
                linear_sums(g)


_OUT = (4, 512, 512)


def kernel(**inputs):
    import numpy as np
    import concourse.bacc as bacc
    from concourse.bass_utils import run_bass_kernel_spmd

    given = {k.replace("L0_", ""): np.asarray(v) for k, v in inputs.items()}
    x = given["attn_hidden_states"].reshape(-1, _OUT[-1])
    H = x.shape[1]
    F = given["attn_ffn_gate_w"].shape[0]
    S, G = given["attn_fuse_weight"].shape[1:]
    pairs = -(-F // (2 * P))
    padded = 2 * P * pairs

    def pad(w):
        return np.concatenate([w, np.zeros((padded - F, H), w.dtype)])

    def by_chunk(w):
        return w.reshape(-1, P, H // P, P).transpose(0, 3, 2, 1).reshape(-1, P, H)

    bank_a = by_chunk(np.concatenate([pad(given["attn_ffn_gate_w"]), given["attn_up_w"]]))
    bank_b = by_chunk(np.concatenate([pad(given["attn_ffn_up_w"]), given["attn_gate_w"]]))
    down = np.concatenate([pad(given["attn_ffn_down_w"].T).reshape(-1, P, H),
                           given["attn_local_approx_output"].T[None],
                           given["attn_fuse_weight"].transpose(2, 1, 0)])
    arrays = {
        "x": x,
        "gate_up_w": np.concatenate([bank_a, bank_b], axis=2),
        "down_w": down,
        "local_point": given["attn_local_point"],
        "discount": given["attn_discount_factor"],
        "q_w": given["ffn_qweight"].T,
        "q_scales": given["ffn_scales"].reshape(H, -1).T,
        "q_zeros": given["ffn_zeros"].reshape(H, -1).T,
        "bias": given["ffn_bias"],
    }
    arrays = {k: np.ascontiguousarray(v) for k, v in arrays.items()}
    nc = bacc.Bacc("TRN2", target_bir_lowering=False, num_devices=1)
    args = [nc.dram_tensor(k, v.shape, mybir.dt.from_np(v.dtype), kind="ExternalInput").ap()
            for k, v in arrays.items()]
    args.append(nc.dram_tensor("out", x.shape, mybir.dt.float32, kind="ExternalOutput").ap())
    block_kernel(nc, *args)
    r = run_bass_kernel_spmd(nc, [arrays], core_ids=[0])
    return r.results[0]["out"].reshape(_OUT)
```

```python
from contextlib import ExitStack

import concourse.bass as bass
from concourse import mybir

P = 128
ALU = mybir.AluOpType
ACT = mybir.ActivationFunctionType
F32 = mybir.dt.float32
F32R = mybir.dt.float32r
I32 = mybir.dt.int32

THD = 2.5
GRAD_ORDER_MIN = 4
EPS = 1e-5
QGROUP = 32


def block_kernel(nc, x, gate_up_w, down_w, local_point, discount, q_w, q_scales, q_zeros, bias, out):
    T, H = x.shape
    TILES = T // P
    GT = 4
    GROUPS = TILES // GT
    GN = GT * P
    K = H // P
    GU_CHUNKS = gate_up_w.shape[0]
    FFN_CHUNKS = GU_CHUNKS - 1
    PAIRS = FFN_CHUNKS // 2
    POWERS = down_w.shape[0] - FFN_CHUNKS
    GUW = K * P
    BRANCH = FFN_CHUNKS
    assert H == GN == 512 and GROUPS == 4 and FFN_CHUNKS % 2 == 0 and POWERS == 7

    TURN1 = [0, GT, 2 * GT, 4 * GT]
    USE_LAST = GROUPS * K + PAIRS * TILES
    USES = 2 * GT

    def use_down(p, g):
        if isinstance(p, int) and p == 0 and g == 0:
            return 3 * GT
        return GROUPS * K + TILES * p + GT * g

    def step(p, g, c):
        return 2 * GROUPS * p + 2 * g + c

    BRANCH_STEP = 2 * GROUPS * PAIRS

    with ExitStack() as ctx:
        def sb(name, shape, dt):
            return ctx.enter_context(nc.sbuf_tensor(name, shape, dt))

        def bank(name):
            return ctx.enter_context(nc.psum_tensor(name, [P, 512], F32))

        def sem(name):
            return ctx.enter_context(nc.semaphore(name))

        X = sb("X", [P, TILES, H], F32)
        xT_hi = sb("xT_hi", [P, K, GROUPS, GN], F32R)
        xT_lo = sb("xT_lo", [P, K, GROUPS, GN], F32R)
        x2T_hi, x2T_lo = xT_hi[:, :, 0, :], xT_lo[:, :, 0, :]
        hT = sb("hT", [P, GROUPS, 2, 2, GN], F32R)
        rT = hT[:, :, :, :, :].rearrange("p g c s n -> p (g c s) n")
        gu_w = sb("gu_w", [P, 2, 2, 2, GUW], F32R)
        d_w = sb("d_w", [P, 2, 2, H], F32R)
        fuse_w = sb("fuse_w", [P, POWERS, 2, H], F32R)
        gu_raw = sb("gu_raw", [P, 2, 2 * GUW], F32)
        d_raw = sb("d_raw", [P, 2, H], F32)
        sg = sb("sg", [P, 2, GN], F32)
        hf = sb("hf", [P, 2, GN], F32)
        xhat = sb("xhat", [P, 2, H], F32)
        bias_sb = sb("bias_sb", [P, H], F32)
        ident = sb("ident", [P, P], F32)
        bn = sb("bn", [P, 2, 6], F32)
        mean_var = sb("mean_var", [P, GT, 2], F32)
        var_eps = sb("var_eps", [P, GT], F32)
        rstd = sb("rstd", [P, GT], F32)
        minus_half = sb("minus_half", [P, 1], F32)
        eps = sb("eps", [P, 1], F32)
        lp = sb("lp", [P, 1], F32)
        disc = sb("disc", [P, POWERS - 1], F32)
        coef = sb("coef", [P, POWERS - 1], F32)
        delta, abs_delta = sg[:, 0, :], sg[:, 1, :]
        power = [hf[:, 0, :], hf[:, 1, :], d_raw[:, 0, :], d_raw[:, 1, :]]
        q_val = gu_raw[:, :, :].rearrange("p s (a n) -> p (s a) n", n=H)
        q_zero, q_scale = xhat[:, 0, :], xhat[:, 1, :]

        def q_split(k, part):
            return gu_w[:, 1, part, k, :] if k < 2 else d_w[:, k - 2, part, :]

        row_bank = [bank(f"row_bank{i}") for i in range(4)]
        bank_a = [bank(f"bank_a{i}") for i in range(2)]
        bank_b = [bank(f"bank_b{i}") for i in range(2)]
        linear_bank = [bank_a[1], bank_b[1]]

        x_loaded = [sem(f"x_loaded{i}") for i in range(GT + GROUPS - 1)]
        params_loaded = sem("params_loaded")
        bias_loaded = sem("bias_loaded")
        gu_loaded = [sem(f"gu_loaded{i}") for i in range(2)]
        d_loaded = [sem(f"d_loaded{i}") for i in range(2)]
        q_loaded = sem("q_loaded")
        ident_step = sem("ident_step")
        ident_ready = sem("ident_ready")
        bn_ready = sem("bn_ready")
        mean_ready = sem("mean_ready")
        var_eps_ready = sem("var_eps_ready")
        rstd_ready = sem("rstd_ready")
        xhat_ready = sem("xhat_ready")
        xhat_turned = sem("xhat_turned")
        row_ready = sem("row_ready")
        row_drained = sem("row_drained")
        linear_done = sem("linear_done")
        linear_read = sem("linear_read")
        xT_hi_ready = sem("xT_hi_ready")
        coef_ready = sem("coef_ready")
        gu_hi = sem("gu_hi")
        gu_lo = sem("gu_lo")
        first_hi = sem("first_hi")
        first_lo = sem("first_lo")
        d_scaled = sem("d_scaled")
        d_hi = sem("d_hi")
        d_lo = sem("d_lo")
        gu_done = sem("gu_done")
        a_read = sem("a_read")
        b_read = sem("b_read")
        h_hi = sem("h_hi")
        h_lo = sem("h_lo")
        abs_ready = sem("abs_ready")
        power_ready = sem("power_ready")
        r_hi = sem("r_hi")
        r_lo_pool = sem("r_lo_pool")
        r_lo_dve = sem("r_lo_dve")
        q_cast = sem("q_cast")
        q_sub = sem("q_sub")
        q_mul = sem("q_mul")
        q_hi = sem("q_hi")
        q_lo = sem("q_lo")
        bias_added = sem("bias_added")
        stored = sem("stored")
        POOL_POWERS = 4
        DVE_POWERS = POWERS - POOL_POWERS
        CHAIN = POWERS

        block = ctx.enter_context(nc.Block())

        def rows(g, i):
            return (g * GT + i) * P

        @block.sync
        def _(sp):
            def load_gu(q, slot):
                sp.dma_start(gu_raw[:, slot, :], gate_up_w[q, :, :]).then_inc(gu_loaded[slot], 16)

            def load_d(q, slot):
                sp.dma_start(d_raw[:, slot, :], down_w[q, :, :]).then_inc(d_loaded[slot], 16)

            def load_x(g):
                sp.dma_start(X[:, g * GT:(g + 1) * GT, :],
                             x[g * GN:(g + 1) * GN, :].rearrange("(t p) n -> p t n", p=P)) \
                    .then_inc(x_loaded[GT + g - 1], 16)

            for i in range(GT):
                sp.dma_start(X[:, i, :], x[i * P:(i + 1) * P, :]).then_inc(x_loaded[i], 16)
            load_gu(0, 0)
            load_gu(1, 1)
            load_x(1)
            load_x(2)
            load_d(0, 0)
            load_d(1, 1)
            load_x(3)
            sp.dma_start(bias_sb[:, :], bias.unsqueeze(0).to_broadcast([P, H])).then_inc(bias_loaded, 16)
            with sp.Fori(0, PAIRS - 1) as p:
                for c in range(2):
                    sp.wait_ge(gu_lo, 2 * p + c + 1)
                    load_gu(2 * p + 2 + c, c)
                for c in range(2):
                    sp.wait_ge(d_lo, 2 * p + c + 1)
                    load_d(2 * p + 2 + c, c)
            sp.wait_ge(gu_lo, FFN_CHUNKS - 1)
            load_gu(BRANCH, 0)
            per = P // QGROUP

            def load_q(k):
                if k == 0:
                    sp.wait_ge(gu_lo, FFN_CHUNKS)
                    sp.wait_ge(row_ready, TURN1[-1] + K)
                else:
                    sp.wait_ge(q_mul, k)
                if k == 2:
                    sp.wait_ge(gu_lo, GU_CHUNKS)
                sp.dma_start(q_val[:, (k + 2) % K, :].bitcast(I32), q_w[k * P:(k + 1) * P, :]) \
                    .then_inc(q_loaded, 16)
                for dst, src in ((q_zero, q_zeros), (q_scale, q_scales)):
                    sp.dma_start(dst, src[k * per:(k + 1) * per, :].unsqueeze(1)
                                 .to_broadcast([per, QGROUP, H])).then_inc(q_loaded, 16)

            for m in range(POWERS):
                q = FFN_CHUNKS + m
                sp.wait_ge(d_lo, q - 1)
                load_d(q, q % 2)
                if m in (2, 4):
                    load_q(m // 2 - 1)
            load_q(2)
            load_q(3)
            with sp.Fori(0, GROUPS) as g:
                for i in range(GT):
                    sp.wait_ge(linear_read, GT * g + i + 1)
                    sp.dma_start(out[bass.ds(rows(g, i), P), :], X[:, g * GT + i, :]).then_inc(stored, 16)
            sp.wait_ge(stored, 16 * TILES)

        @block.gpsimd
        def _(pool):
            pool.memset(ident[:, :], 0.0).then_inc(ident_step, 1)
            pool.memset(minus_half[:, :], -0.5).then_inc(ident_step, 1)
            pool.memset(eps[:, :], EPS).then_inc(ident_step, 1)
            pool.wait_ge(ident_step, 3)
            pool.affine_select(out=ident[:, :], in_=ident[:, :], compare_op=ALU.not_equal, fill=1.0,
                               base=0, pattern=[[-1, P]], channel_multiplier=1).then_inc(ident_ready, 1)

            def inv_std(n, i):
                pool.wait_ge(mean_ready, n + 1)
                if not (isinstance(n, int) and n < GT):
                    pool.wait_ge(xhat_ready, n - GT + 1)
                pool.tensor_tensor(var_eps[:, i:i + 1], mean_var[:, i, 1:2], eps[:, :], ALU.add) \
                    .then_inc(var_eps_ready, 1)
                pool.wait_ge(var_eps_ready, n + 1)
                pool.tensor_tensor(rstd[:, i:i + 1], var_eps[:, i:i + 1], minus_half[:, :], ALU.pow) \
                    .then_inc(rstd_ready, 1)

            def split_lo(dst, src, hi):
                return pool.tensor_tensor(dst, src, hi.bitcast(F32), ALU.subtract)

            def split_gu(q, slot):
                pool.wait_ge(gu_hi, q + 1)
                split_lo(gu_w[:, slot, 1, :, :].rearrange("p a n -> p (a n)"), gu_raw[:, slot, :],
                         gu_w[:, slot, 0, :, :].rearrange("p a n -> p (a n)")).then_inc(gu_lo, 1)

            def split_d(q, slot):
                pool.wait_ge(d_hi, q + 1)
                split_lo(d_w[:, slot, 1, :], d_raw[:, slot, :], d_w[:, slot, 0, :]).then_inc(d_lo, 1)

            for g in range(GROUPS):
                for i in range(GT):
                    inv_std(g * GT + i, i)
                if g == 0:
                    for half, step_done in ((0, first_lo), (1, gu_lo)):
                        pool.wait_ge(first_hi if half == 0 else gu_hi, 1)
                        split_lo(gu_w[:, 0, 1, half, :], gu_raw[:, 0, half * GUW:(half + 1) * GUW],
                                 gu_w[:, 0, 0, half, :]).then_inc(step_done, 1)
                    split_gu(1, 1)
                if g == 2:
                    split_d(0, 0)
                    split_d(1, 1)
            split_gu(2, 0)
            split_gu(3, 1)
            with pool.Fori(1, PAIRS - 1) as p:
                for c in range(2):
                    split_d(2 * p + c, c)
                for c in range(2):
                    split_gu(2 * p + 2 + c, c)
            for c in range(2):
                split_d(FFN_CHUNKS - 2 + c, c)

            def dequantise(k):
                w = q_val[:, (k + 2) % K, :]
                pool.wait_ge(q_cast, k + 1)
                pool.tensor_tensor(w, w, q_zero, ALU.subtract).then_inc(q_sub, 1)
                pool.wait_ge(q_sub, k + 1)
                pool.tensor_tensor(w, w, q_scale, ALU.mult).then_inc(q_mul, 1)

            def split_linear(k):
                pool.wait_ge(q_hi, k + 1)
                split_lo(q_split(k, 1), q_val[:, (k + 2) % K, :], q_split(k, 0)).then_inc(q_lo, 1)

            for m in range(POWERS):
                q = FFN_CHUNKS + m
                if m >= 1:
                    pool.wait_ge(d_loaded[q % 2], 16 * (q // 2 + 1))
                    if m == 1:
                        pool.wait_ge(coef_ready, 1)
                    pool.tensor_scalar(d_raw[:, q % 2, :], d_raw[:, q % 2, :], coef[:, m - 1:m], None,
                                       ALU.mult).then_inc(d_scaled, 1)
                if m == POWERS - 2:
                    split_gu(BRANCH, 0)
                if m in (3, 4):
                    dequantise(m - 3)
                pool.wait_ge(d_hi, q + 1)
                split_lo(fuse_w[:, m, 1, :], d_raw[:, q % 2, :], fuse_w[:, m, 0, :]).then_inc(d_lo, 1)

            def split_powers(g):
                for m in range(POOL_POWERS):
                    pool.wait_ge(r_hi, POWERS * g + m + 1)
                    split_lo(rT[:, 2 * m + 1, :], power[m], rT[:, 2 * m, :]).then_inc(r_lo_pool, 1)

            def add_bias(g, i):
                pool.wait_ge(xhat_ready, TILES + GT * g + i + 1)
                pool.tensor_tensor(X[:, g * GT + i, :], X[:, g * GT + i, :], bias_sb[:, :], ALU.add) \
                    .then_inc(bias_added, 1)

            split_powers(0)
            pool.wait_ge(bias_loaded, 16)
            dequantise(2)
            dequantise(3)
            for i in range(GT):
                inv_std(TILES + i, i)
                split_linear(i)
            for i in range(GT):
                add_bias(0, i)
            split_powers(1)
            with pool.Fori(1, GROUPS - 1) as g:
                for i in range(GT):
                    inv_std(TILES + GT * g + i, i)
                for i in range(GT):
                    add_bias(g, i)
                split_powers(g + 1)
            for i in range(GT):
                inv_std(TILES + GT * (GROUPS - 1) + i, i)
            for i in range(GT):
                add_bias(GROUPS - 1, i)

        @block.scalar
        def _(act):
            act.dma_start(disc[:, :], discount.unsqueeze(0).to_broadcast([P, POWERS - 1])) \
                .then_inc(params_loaded, 16)
            act.dma_start(lp[:, :], local_point.unsqueeze(1)).then_inc(params_loaded, 16)
            act.wait_ge(params_loaded, 32)
            act.activation(coef[:, :], disc[:, :], ACT.Exp, scale=-1.0).then_inc(coef_ready, 1)
            act.wait_ge(gu_loaded[0], 16)
            for half, step_done in ((0, first_hi), (1, gu_hi)):
                act.activation(gu_w[:, 0, 0, half, :], gu_raw[:, 0, half * GUW:(half + 1) * GUW],
                               ACT.Copy).then_inc(step_done, 1)

            def split_gu(q, slot, loads, steps_done):
                act.wait_ge(gu_loaded[slot], 16 * loads)
                if steps_done is not None:
                    act.wait_ge(gu_done, steps_done)
                act.activation(gu_w[:, slot, 0, :, :].rearrange("p a n -> p (a n)"), gu_raw[:, slot, :],
                               ACT.Copy).then_inc(gu_hi, 1)

            def split_d(slot, loads, uses_done):
                act.wait_ge(d_loaded[slot], 16 * loads)
                if uses_done is not None:
                    act.wait_ge(row_ready, uses_done)
                act.activation(d_w[:, slot, 0, :], d_raw[:, slot, :], ACT.Copy).then_inc(d_hi, 1)

            def split_fuse(m):
                q = FFN_CHUNKS + m
                if m == 0:
                    act.wait_ge(d_loaded[q % 2], 16 * (q // 2 + 1))
                else:
                    act.wait_ge(d_scaled, m)
                act.activation(fuse_w[:, m, 0, :], d_raw[:, q % 2, :], ACT.Copy).then_inc(d_hi, 1)

            def xT_hi_group(use, dst):
                for k in range(K):
                    act.wait_ge(row_ready, use + k + 1)
                    act.activation(dst[k], row_bank[k][:, :], ACT.Copy).then_inc(xT_hi_ready, 1)

            def ffn_step(n, g, c, uses_done):
                act.wait_ge(gu_done, n + 1)
                if not (isinstance(n, int) and n < 2):
                    act.wait_ge(b_read, n - 1)
                act.activation(sg[:, c, :], bank_a[c][:, :], ACT.Silu).then_inc(a_read, 1)
                act.wait_ge(b_read, n + 1)
                if uses_done is not None:
                    act.wait_ge(row_ready, uses_done)
                act.activation(hT[:, g, c, 0, :], hf[:, c, :], ACT.Copy).then_inc(h_hi, 1)

            def xT_hi_of(g):
                xT_hi_group(TURN1[g], [xT_hi[:, k, g, :] for k in range(K)])

            def h_free(p, g):
                if isinstance(p, int) and p == 0:
                    return None
                return TILES * p + (GROUPS * K - TILES + GT * (g + 1))

            def pair(p, after):
                for g in range(GROUPS):
                    for c in range(2):
                        ffn_step(step(p, g, c), g, c, h_free(p, g))
                        after(g, c)

            xT_hi_of(0)
            split_gu(1, 1, 1, None)

            def after_first(g, c):
                if c == 0 and g + 1 < GROUPS:
                    xT_hi_of(g + 1)
                if (g, c) == (0, 1):
                    split_d(0, 1, None)
                    split_d(1, 1, None)
                if g == GROUPS - 1:
                    split_gu(2 + c, c, 2, step(0, g, c) + 1)

            pair(0, after_first)

            with act.Fori(1, PAIRS - 1) as p:
                def after(g, c):
                    if (g, c) == (0, 0):
                        for slot in range(2):
                            split_d(slot, p + 1, GROUPS * K + TILES * p)
                    if g == GROUPS - 1:
                        split_gu(2 * p + 2 + c, c, p + 2, step(p, g, c) + 1)
                pair(p, after)

            def cast_linear(k):
                act.wait_ge(q_loaded, 48 * (k + 1))
                w = q_val[:, (k + 2) % K, :]
                act.activation(w, w.bitcast(I32), ACT.Copy).then_inc(q_cast, 1)

            def after_last(g, c):
                if (g, c) == (0, 0):
                    for slot in range(2):
                        split_d(slot, PAIRS, USE_LAST - TILES)
                    return
                if (g, c) == (GROUPS - 1, 0):
                    split_gu(BRANCH, 0, PAIRS + 1, step(PAIRS - 1, g, 0) + 1)
                split_fuse(2 * g + c - 1)
                if 2 * g + c in (3, 4):
                    cast_linear(2 * g + c - 3)

            pair(PAIRS - 1, after_last)

            def copy_up(g):
                act.wait_ge(gu_done, BRANCH_STEP + g + 1)
                if isinstance(g, int) and g == 0:
                    act.wait_ge(h_lo, BRANCH_STEP)
                else:
                    act.wait_ge(power_ready, CHAIN * g)
                    act.wait_ge(r_lo_dve, DVE_POWERS * g)
                    act.wait_ge(r_lo_pool, POOL_POWERS * g)
                act.activation(power[0], bank_a[0][:, :], ACT.Copy).then_inc(a_read, 1)

            def powers_hi(g, first):
                for m in range(POWERS):
                    if first and m == POWERS - 1:
                        cast_linear(2)
                    if m == 0:
                        act.wait_ge(a_read, BRANCH_STEP + g + 1)
                    elif m == 1:
                        act.wait_ge(b_read, BRANCH_STEP + g + 1)
                        act.activation(abs_delta, delta, ACT.Abs).then_inc(abs_ready, 1)
                        act.wait_ge(power_ready, CHAIN * g + 1)
                    else:
                        act.wait_ge(power_ready, CHAIN * g + (m if m <= GRAD_ORDER_MIN else m + 1))
                    if first:
                        act.wait_ge(row_ready, USE_LAST - TILES + GT * (m // 2 + 1))
                    elif m == 0:
                        act.wait_ge(row_ready, USES * g + (USE_LAST - USES + GT))
                    act.activation(rT[:, 2 * m, :], power[m % 4 if m <= GRAD_ORDER_MIN else m - 3],
                                   ACT.Copy).then_inc(r_hi, 1)

            def linear_hi(k):
                act.wait_ge(q_mul, k + 1)
                if k == 0:
                    act.wait_ge(gu_done, BRANCH_STEP)
                if k == 2:
                    act.wait_ge(row_ready, USE_LAST)
                act.activation(q_split(k, 0), q_val[:, (k + 2) % K, :], ACT.Copy).then_inc(q_hi, 1)

            def x2T_hi_group(g):
                xT_hi_group(USE_LAST + USES * g + GT, [x2T_hi[:, k, :] for k in range(K)])

            copy_up(0)
            powers_hi(0, True)
            cast_linear(3)
            for k in range(K):
                linear_hi(k)
            act.wait_ge(gu_done, BRANCH_STEP + 1)
            x2T_hi_group(0)
            copy_up(1)
            powers_hi(1, False)
            with act.Fori(1, GROUPS - 1) as g:
                act.wait_ge(linear_done, GT * g)
                x2T_hi_group(g)
                copy_up(g + 1)
                powers_hi(g + 1, False)
            act.wait_ge(linear_done, GT * (GROUPS - 1))
            x2T_hi_group(GROUPS - 1)

        @block.tensor
        def _(pe):
            def product(ps, pairs, k_first, k_last, done, lo_written=None):
                for j, (a, b) in enumerate(pairs):
                    if j == 2 and lo_written is not None:
                        pe.wait_ge(row_drained, lo_written)
                    mm = pe.matmul(ps, a, b, start=(k_first and j == 0),
                                   stop=(k_last and j == len(pairs) - 1))
                if done is not None:
                    mm.then_inc(done, 1)

            def gate_up(n, slot, g, bank, first_wait, xT_wait, banks_read, hook):
                first_chunk = isinstance(n, int) and n == 0
                if first_wait is not None and not first_chunk:
                    pe.wait_ge(gu_lo, first_wait)
                if banks_read is not None:
                    pe.wait_ge(a_read, banks_read)
                    pe.wait_ge(b_read, banks_read)
                for b, ps in enumerate((bank_a[bank], bank_b[bank])):
                    for k in range(K):
                        if first_chunk and k == 0:
                            pe.wait_ge(gu_lo if b else first_lo, 1)
                        new = xT_wait and b == 0
                        if new:
                            pe.wait_ge(xT_hi_ready, K * g + k + 1)
                        w_hi = gu_w[:, slot, 0, b, k * P:(k + 1) * P]
                        w_lo = gu_w[:, slot, 1, b, k * P:(k + 1) * P]
                        x_hi, x_lo = xT_hi[:, k, g, :], xT_lo[:, k, g, :]
                        last = b == 1 and k == K - 1
                        product(ps[:, :], [(w_hi, x_hi), (w_lo, x_hi), (w_hi, x_lo)], k == 0, k == K - 1,
                                gu_done if last else None, TURN1[g] + k + 1 if new else None)
                        hook(b * K + k)

            def turn(use, tile, i):
                pe.wait_ge(xhat_ready, tile + 1)
                if i == 0 and not (isinstance(use, int) and use == 0):
                    pe.wait_ge(row_drained, use)
                for k in range(K):
                    mm = pe.transpose(row_bank[k][:, i * P:(i + 1) * P], xhat[:, i % 2, k * P:(k + 1) * P],
                                      ident[:, :])
                    if i == GT - 1:
                        mm.then_inc(row_ready, 1)
                if i < GT - 1:
                    mm.then_inc(xhat_turned, 1)

            def no_hook(j):
                pass

            def down(p, g):
                for i in range(GT):
                    use = use_down(p, g) + i
                    if i == 0:
                        pe.wait_ge(h_lo, step(p, g, 1) + 1)
                        if g == 0:
                            pe.wait_ge(d_lo, 2 * p + 2)
                    pe.wait_ge(row_drained, use - 3)
                    for c in range(2):
                        a_hi = hT[:, g, c, 0, i * P:(i + 1) * P]
                        a_lo = hT[:, g, c, 1, i * P:(i + 1) * P]
                        product(row_bank[i][:, :], [(a_hi, d_w[:, c, 0, :]), (a_hi, d_w[:, c, 1, :]),
                                                    (a_lo, d_w[:, c, 0, :])], c == 0, c == 1,
                                row_ready if c == 1 else None)

            def fuse(g):
                if isinstance(g, int) and g == 0:
                    pe.wait_ge(d_lo, FFN_CHUNKS + POWERS)
                for i in range(GT):
                    pe.wait_ge(row_drained, USE_LAST + USES * g + i - 3)
                    for m in range(POWERS):
                        if i == 0:
                            if m < POOL_POWERS:
                                pe.wait_ge(r_lo_pool, POOL_POWERS * g + m + 1)
                            else:
                                pe.wait_ge(r_lo_dve, DVE_POWERS * g + m - POOL_POWERS + 1)
                        a_hi = rT[:, 2 * m, i * P:(i + 1) * P]
                        a_lo = rT[:, 2 * m + 1, i * P:(i + 1) * P]
                        last = m == POWERS - 1
                        product(row_bank[i][:, :], [(a_hi, fuse_w[:, m, 0, :]), (a_hi, fuse_w[:, m, 1, :]),
                                                    (a_lo, fuse_w[:, m, 0, :])], m == 0, last,
                                row_ready if last else None)

            def linear(g, tiles):
                for i in tiles:
                    n = GT * g + i
                    if not (isinstance(g, int) and g == 0 and i < 2):
                        pe.wait_ge(linear_read, n - 1)
                    for k in range(K):
                        if i == 0:
                            pe.wait_ge(xT_hi_ready, K * (GROUPS + g) + k + 1)
                        a_hi = x2T_hi[:, k, i * P:(i + 1) * P]
                        a_lo = x2T_lo[:, k, i * P:(i + 1) * P]
                        w_hi, w_lo = q_split(k, 0), q_split(k, 1)
                        product(linear_bank[i % 2][:, :], [(a_hi, w_hi), (a_hi, w_lo), (a_lo, w_hi)],
                                k == 0, k == K - 1, linear_done if k == K - 1 else None,
                                USE_LAST + USES * g + GT + k + 1 if i == 0 else None)

            pe.wait_ge(ident_ready, 1)
            for i in range(GT):
                turn(0, i, i)

            def pair(p):
                for g in range(GROUPS):
                    for c in range(2):
                        first = isinstance(p, int) and p == 0

                        def hook(j):
                            j = 2 * K * c + j
                            if first and g + 1 < GROUPS and j in TURN_AFTER:
                                i = TURN_AFTER.index(j)
                                turn(TURN1[g + 1], (g + 1) * GT + i, i)
                        gate_up(step(p, g, c), c, g, c, 2 * p + c + 1 if g == 0 else None,
                                first and c == 0, None if first and g == 0 else step(p, g, c) - 1, hook)
                    if g in (1, 2):
                        down(p, g - 1)
                if isinstance(p, int) and p == PAIRS - 1:
                    gate_up(BRANCH_STEP, 0, 0, 0, GU_CHUNKS, False, BRANCH_STEP - 1, no_hook)
                down(p, GROUPS - 2)
                down(p, GROUPS - 1)

            TURN_AFTER = [7, 9, 11, 13]
            pair(0)
            with pe.Fori(1, PAIRS - 1) as p:
                pair(p)
            pair(PAIRS - 1)

            def turn2(g, i):
                turn(USE_LAST + USES * g + GT, TILES + GT * g + i, i)

            def last_stage(g):
                first = isinstance(g, int) and g == 0
                fuse(g)
                if not first:
                    linear(g - 1, [GT - 1])

                def hook(j):
                    if j in TURN2_AFTER:
                        turn2(g, TURN2_AFTER.index(j))
                gate_up(BRANCH_STEP + g + 1, 0, g + 1, 0, None, False, BRANCH_STEP + g + 1, hook)
                if first:
                    pe.wait_ge(q_lo, K)
                linear(g, range(GT - 1))

            TURN2_AFTER = [1, 2, 4, 5]
            last_stage(0)
            with pe.Fori(1, GROUPS - 1) as g:
                last_stage(g)
            fuse(GROUPS - 1)
            linear(GROUPS - 2, [GT - 1])
            for i in range(GT):
                turn2(GROUPS - 1, i)
            linear(GROUPS - 1, range(GT))

        @block.vector
        def _(dve):
            def stats(n, tile, i):
                if not (isinstance(n, int) and n < 2):
                    dve.wait_ge(mean_ready, n - 1)
                dve.bn_stats(bn[:, i % 2, :], X[:, tile, :]).then_inc(bn_ready, 1)
                dve.wait_ge(bn_ready, n + 1)
                if not (isinstance(n, int) and n < GT):
                    dve.wait_ge(xhat_ready, n - GT + 1)
                    dve.wait_ge(var_eps_ready, n - GT + 1)
                dve.bn_aggr(mean_var[:, i, :], bn[:, i % 2, :]).then_inc(mean_ready, 1)

            def normalise(n, tile, i, turned, use_before):
                dve.wait_ge(rstd_ready, n + 1)
                if isinstance(n, int) and n == TILES:
                    dve.wait_ge(q_mul, K)
                if turned is not None:
                    dve.wait_ge(xhat_turned, turned)
                if use_before is not None:
                    dve.wait_ge(row_ready, use_before)
                dve.tensor_scalar(xhat[:, i % 2, :], X[:, tile, :], mean_var[:, i, 0:1], rstd[:, i:i + 1],
                                  ALU.subtract, ALU.mult).then_inc(xhat_ready, 1)

            def xT_lo_group(use, hi, dst, src):
                for k in range(K):
                    dve.wait_ge(xT_hi_ready, hi + k + 1)
                    dve.tensor_tensor(dst[k], row_bank[k][:, :], src[k].bitcast(F32), ALU.subtract) \
                        .then_inc(row_drained, 1)

            def ffn_h(n, g, c):
                dve.wait_ge(a_read, n + 1)
                if not (isinstance(n, int) and n < 2):
                    dve.wait_ge(h_hi, n - 1)
                    dve.wait_ge(h_lo, n - 1)
                dve.tensor_tensor(hf[:, c, :], bank_b[c][:, :], sg[:, c, :], ALU.mult) \
                    .then_inc(b_read, 1)
                dve.wait_ge(h_hi, n + 1)
                dve.wait_ge(b_read, n + 1)
                dve.tensor_tensor(hT[:, g, c, 1, :], hf[:, c, :], hT[:, g, c, 0, :].bitcast(F32),
                                  ALU.subtract).then_inc(h_lo, 1)

            def accumulate(use, tile, i):
                dve.wait_ge(row_ready, use + 1)
                dve.wait_ge(row_drained, use)
                dve.tensor_tensor(X[:, tile, :], row_bank[i][:, :], X[:, tile, :], ALU.add) \
                    .then_inc(row_drained, 1)

            def norm1(g):
                for i in range(GT + 1):
                    if i < GT:
                        n = g * GT + i
                        if g == 0 or i == 0:
                            dve.wait_ge(x_loaded[i if g == 0 else GT + g - 1], 16)
                        stats(n, n, i)
                    if i >= 1:
                        n = g * GT + i - 1
                        turned = use_before = None
                        if i - 1 >= 2:
                            turned = 3 * g + i - 2
                        elif g >= 1:
                            turned = 3 * g
                            use_before = TURN1[g - 1] + K if i - 1 == 1 else None
                        normalise(n, n, i - 1, turned, use_before)

            def norm1_turned(g):
                xT_lo_group(TURN1[g], K * g, [xT_lo[:, k, g, :] for k in range(K)],
                            [xT_hi[:, k, g, :] for k in range(K)])

            def down_sums(p, g):
                for i in range(GT):
                    accumulate(use_down(p, g) + i, GT * g + i, i)

            def pair(p):
                first, last = (isinstance(p, int) and p == q for q in (0, PAIRS - 1))
                for g in range(GROUPS):
                    if first and g + 1 < GROUPS:
                        norm1(g + 1)
                    ffn_h(step(p, g, 0), g, 0)
                    if first and g + 1 < GROUPS:
                        norm1_turned(g + 1)
                    ffn_h(step(p, g, 1), g, 1)
                    if g in (1, 2):
                        down_sums(p, g - 1)
                if last:
                    def sums(j):
                        if j in (1, 3, 5, 6):
                            i = (1, 3, 5, 6).index(j)
                            accumulate(use_down(p, 2) + i, 2 * GT + i, i)
                    chain(0, sums)
                    powers_lo(0, [4, 5])
                else:
                    down_sums(p, 2)
                down_sums(p, 3)
                if last:
                    powers_lo(0, [6])

            norm1(0)
            norm1_turned(0)

            def chain(g, hook=None):
                n = BRANCH_STEP + g
                dve.wait_ge(gu_done, n + 1)
                first = isinstance(g, int) and g == 0
                if first:
                    dve.wait_ge(params_loaded, 32)
                    dve.wait_ge(b_read, n)
                else:
                    dve.wait_ge(power_ready, CHAIN * g)
                dve.tensor_scalar(delta, bank_b[0][:, :], lp[:, 0:1], None, ALU.subtract) \
                    .then_inc(b_read, 1)
                dve.wait_ge(b_read, n + 1)
                for j in range(CHAIN):
                    if j == 0:
                        dve.wait_ge(a_read, n + 1)
                    else:
                        dve.wait_ge(power_ready, CHAIN * g + j)
                    src = power[j % 4]
                    dst = power[(j + 1) % 4]
                    if j < 3:
                        if first and j == 0:
                            dve.wait_ge(h_lo, n)
                            dve.wait_ge(h_hi, n)
                        if first and j == 1:
                            dve.wait_ge(d_lo, FFN_CHUNKS + POWERS)
                        if not first and j == 0:
                            dve.wait_ge(r_hi, POWERS * g)
                            dve.wait_ge(r_lo_pool, POOL_POWERS * g)
                            dve.wait_ge(r_lo_dve, DVE_POWERS * g)
                    else:
                        dve.wait_ge(r_hi, POWERS * g + j - 2)
                        dve.wait_ge(r_lo_pool, POOL_POWERS * g + j - 2)
                    if j == GRAD_ORDER_MIN:
                        dve.wait_ge(abs_ready, g + 1)
                        dve.scalar_tensor_tensor(out=dst, in0=abs_delta, scalar=THD, in1=src,
                                                 op0=ALU.is_le, op1=ALU.mult).then_inc(power_ready, 1)
                    else:
                        dve.tensor_tensor(dst, src, delta, ALU.mult).then_inc(power_ready, 1)
                    if hook is not None:
                        hook(j)

            def powers_lo(g, which):
                for m in which:
                    dve.wait_ge(r_hi, POWERS * g + m + 1)
                    dve.tensor_tensor(rT[:, 2 * m + 1, :], power[m % 4 if m <= GRAD_ORDER_MIN else m - 3],
                                      rT[:, 2 * m, :].bitcast(F32), ALU.subtract).then_inc(r_lo_dve, 1)

            pair(0)
            with dve.Fori(1, PAIRS - 1) as p:
                pair(p)
            pair(PAIRS - 1)

            def linear_sum(g, i):
                dve.wait_ge(linear_done, GT * g + i + 1)
                dve.wait_ge(bias_added, GT * g + i + 1)
                dve.tensor_tensor(X[:, GT * g + i, :], linear_bank[i % 2][:, :], X[:, GT * g + i, :],
                                  ALU.add).then_inc(linear_read, 1)

            for g in range(GROUPS):
                use = USE_LAST + USES * g
                for i in range(GT + 1):
                    if i < GT:
                        accumulate(use + i, GT * g + i, i)
                        dve.wait_ge(row_drained, use + i + 1)
                        stats(TILES + GT * g + i, GT * g + i, i)
                    if i >= 1:
                        turned = 3 * (GROUPS + g) + (i - 2 if i - 1 >= 2 else 0)
                        before = None
                        if i - 1 == 1:
                            before = use if g >= 1 else TURN1[-1] + K
                        normalise(TILES + GT * g + i - 1, GT * g + i - 1, i - 1, turned, before)
                if g >= 1:
                    linear_sum(g - 1, GT - 1)
                xT_lo_group(use + GT, K * (GROUPS + g), [x2T_lo[:, k, :] for k in range(K)],
                            [x2T_hi[:, k, :] for k in range(K)])
                if g + 1 < GROUPS:
                    def sums(j):
                        if j in (2, 5):
                            linear_sum(g, (2, 5).index(j))
                    chain(g + 1, sums)
                    powers_lo(g + 1, [4, 5, 6])
                    linear_sum(g, 2)
                else:
                    for i in range(GT - 1):
                        linear_sum(g, i)
            linear_sum(GROUPS - 1, GT - 1)


_OUT = (4, 512, 512)


def kernel(**inputs):
    import numpy as np
    import concourse.bacc as bacc
    from concourse.bass_utils import run_bass_kernel_spmd

    given = {k.replace("L0_", ""): np.asarray(v) for k, v in inputs.items()}
    x = given["attn_hidden_states"].reshape(-1, _OUT[-1])
    H = x.shape[1]
    F = given["attn_ffn_gate_w"].shape[0]
    S, G = given["attn_fuse_weight"].shape[1:]
    pairs = -(-F // (2 * P))
    padded = 2 * P * pairs

    def pad(w):
        return np.concatenate([w, np.zeros((padded - F, H), w.dtype)])

    def by_chunk(w):
        return w.reshape(-1, P, H // P, P).transpose(0, 3, 2, 1).reshape(-1, P, H)

    bank_a = by_chunk(np.concatenate([pad(given["attn_ffn_gate_w"]), given["attn_up_w"]]))
    bank_b = by_chunk(np.concatenate([pad(given["attn_ffn_up_w"]), given["attn_gate_w"]]))
    down = np.concatenate([pad(given["attn_ffn_down_w"].T).reshape(-1, P, H),
                           given["attn_local_approx_output"].T[None],
                           given["attn_fuse_weight"].transpose(2, 1, 0)])
    arrays = {
        "x": x,
        "gate_up_w": np.concatenate([bank_a, bank_b], axis=2),
        "down_w": down,
        "local_point": given["attn_local_point"],
        "discount": given["attn_discount_factor"],
        "q_w": given["ffn_qweight"].T,
        "q_scales": given["ffn_scales"].reshape(H, -1).T,
        "q_zeros": given["ffn_zeros"].reshape(H, -1).T,
        "bias": given["ffn_bias"],
    }
    arrays = {k: np.ascontiguousarray(v) for k, v in arrays.items()}
    nc = bacc.Bacc("TRN2", target_bir_lowering=False, num_devices=1)
    args = [nc.dram_tensor(k, v.shape, mybir.dt.from_np(v.dtype), kind="ExternalInput").ap()
            for k, v in arrays.items()]
    args.append(nc.dram_tensor("out", x.shape, mybir.dt.float32, kind="ExternalOutput").ap())
    block_kernel(nc, *args)
    r = run_bass_kernel_spmd(nc, [arrays], core_ids=[0])
    return r.results[0]["out"].reshape(_OUT)
```
